# Optimizing a Trainium2 kernel written in Bass

```python
import numpy as np
import jax
import jax.numpy as jnp

def _softmax(x, axis=-1):
    return jax.nn.softmax(x, axis=axis)

def _gelu(x):
    return jax.nn.gelu(x, approximate=True)

def _silu(x):
    return jax.nn.silu(x)

def _sigmoid(x):
    return jax.nn.sigmoid(x)

def _layernorm(x, axis=-1, eps=1e-05):
    m = jnp.mean(x, axis=axis, keepdims=True)
    v = jnp.var(x, axis=axis, keepdims=True)
    return (x - m) / jnp.sqrt(v + eps)

def _scatter_add(tgt, idx, src, axis=0):
    return tgt.at[idx].add(src)

def _segment_sum(src, seg, n):
    return jax.ops.segment_sum(src, seg, n)
kernel_name = 'mk_adj_resnorm_d1_adj_r2_9e2533'

def setup_inputs(seed: int=0):
    np.random.seed(seed)
    _w = jnp.asarray

    def _rec_inputs():
        import jax
        import jax.numpy as jnp
        _gk = jax.random.key(seed)
        x = -0.0002928 + 1 * jax.random.normal(jax.random.fold_in(_gk, 1), (4096, 256), jnp.float32)
        _a = jax.random.bernoulli(jax.random.fold_in(_gk, 2), 0.00195312, (4096, 4096))
        _a = jnp.logical_or(_a, jnp.eye(4096, dtype=bool))
        _af = _a.astype(jnp.float32)
        _af = _af / jnp.maximum(_af.sum(-1, keepdims=True), 1.0)
        adj = _af
        return (x, adj)
    x, adj = _rec_inputs()

    def _L0_gnn_setup():
        import jax, jax.numpy as jnp
        import numpy as np
        N = 4096
        D = 256
        H = 256

        def _graph_conv(feats, adj, W, b):
            agg = adj @ feats
            cat = jnp.concatenate([feats, agg], axis=-1)
            return jax.nn.relu(jnp.einsum('nd,df->nf', cat, W) + b)
        key = jax.random.key(seed)
        k1, k2, k3, k4 = jax.random.split(key, 4)
        x = jax.random.normal(k1, (N, D), dtype=jnp.float32)
        adj = jax.random.uniform(k2, (N, N), dtype=jnp.float32)
        adj = adj / jnp.sum(adj, axis=-1, keepdims=True)
        lim1 = float(np.sqrt(6.0 / (2 * D + H)))
        lim2 = float(np.sqrt(6.0 / (2 * H + H)))
        W1 = jax.random.uniform(k3, (2 * D, H), dtype=jnp.float32, minval=-lim1, maxval=lim1)
        W2 = jax.random.uniform(k4, (2 * H, H), dtype=jnp.float32, minval=-lim2, maxval=lim2)
        b1 = jnp.zeros((H,), dtype=jnp.float32)
        b2 = jnp.zeros((H,), dtype=jnp.float32)
        return {'x': x, 'adj': adj, 'W1': W1, 'b1': b1, 'W2': W2, 'b2': b2}
    _L0_gnn_all = _L0_gnn_setup()
    _L0_gnn_in = {k: v for k, v in _L0_gnn_all.items() if k in ('W1', 'b1', 'W2', 'b2')}
    del _L0_gnn_all
    return {'x': x, 'adj': adj, 'L0_gnn_W1': _L0_gnn_in['W1'], 'L0_gnn_b1': _L0_gnn_in['b1'], 'L0_gnn_W2': _L0_gnn_in['W2'], 'L0_gnn_b2': _L0_gnn_in['b2']}

def reference(x, adj, L0_gnn_W1, L0_gnn_b1, L0_gnn_W2, L0_gnn_b2):
    import jax
    import jax.numpy as jnp

    def _L0_gnn_ref(x, adj, W1, b1, W2, b2):
        import jax, jax.numpy as jnp
        import numpy as np
        N = 4096
        D = 256
        H = 256

        def _graph_conv(feats, adj, W, b):
            agg = adj @ feats
            cat = jnp.concatenate([feats, agg], axis=-1)
            return jax.nn.relu(jnp.einsum('nd,df->nf', cat, W) + b)
        h = _graph_conv(x, adj, W1, b1)
        out = jax.nn.relu(_graph_conv(h, adj, W2, b2) + h)
        return out
    x = _layernorm(x + _L0_gnn_ref(x, adj, L0_gnn_W1, L0_gnn_b1, L0_gnn_W2, L0_gnn_b2), axis=-1)
    return x

_drawn_inputs = setup_inputs


def setup_inputs(seed=0):
    import zlib

    import numpy as np

    out = dict(_drawn_inputs(seed))
    spreads = {'L0_gnn_b1': (0.0, 0.1), 'L0_gnn_b2': (0.0, 0.1)}
    factors = {}
    for name, (base, spread) in spreads.items():
        noise = np.random.default_rng([zlib.crc32(name.encode()), seed]).standard_normal(out[name].shape)
        drawn = base * np.exp(spread * noise) if base else spread * noise
        out[name] = jnp.asarray(drawn.astype(out[name].dtype))
    for name, factor in factors.items():
        out[name] = (out[name] * factor).astype(out[name].dtype)
    return out
```

```python
from contextlib import ExitStack

import concourse.bass as bass
from concourse import mybir


F32 = mybir.dt.float32
F32R = mybir.dt.float32r
ALU = mybir.AluOpType
ACT = mybir.ActivationFunctionType

P = 128
BLOCK = 512
CK = 2
EPS = 1e-5


def graph_resnorm_kernel(nc, adj_t, x_t, w1, w2, b1, b2, ident, h_t, out):
    BLOCKS, CHUNKS = adj_t.shape[:2]
    KT = CHUNKS * CK
    HALVES = x_t.shape[2]
    D = HALVES * P
    TILES = BLOCK // P
    RING = 4
    assert HALVES * BLOCK == CK * BLOCK and CHUNKS % RING == 0 and BLOCKS % RING == 0
    CPB = CHUNKS // BLOCKS
    EVAC_AT = RING - 2
    ROWS_AT = 4
    SELF_AT = 11
    STORE_AT = 9

    with ExitStack() as ctx:
        def sb(name, shape, dt=F32, where=ctx):
            return where.enter_context(nc.sbuf_tensor(name, shape, dt))

        def sem(name):
            return ctx.enter_context(nc.semaphore(name))

        raw = [sb(f"raw{i}", [P, CK, BLOCK]) for i in range(RING)]
        chunk_hi = [sb(f"chunk_hi{i}", [P, CK, BLOCK], F32R) for i in range(RING)]
        chunk_lo = [sb(f"chunk_lo{i}", [P, CK, BLOCK], F32R) for i in range(RING)]
        w_raw = sb("w_raw", [P, HALVES, D])
        w_hi = [sb(f"w_hi{i}", [P, HALVES, D], F32R) for i in range(2)]
        w_lo = [sb(f"w_lo{i}", [P, HALVES, D], F32R) for i in range(2)]
        feat_raw = sb("feat_raw", [P, HALVES, BLOCK])
        feat_hi = sb("feat_hi", [P, HALVES, BLOCK], F32R)
        feat_lo = sb("feat_lo", [P, HALVES, BLOCK], F32R)
        act_t = sb("act_t", [P, HALVES, BLOCK])
        bias1 = sb("bias1", [P, HALVES])
        bias2 = sb("bias2", [P, HALVES])
        identity = sb("identity", [P, P])
        stats = sb("stats", [P, TILES, 6])
        mean = sb("mean", [P, TILES])
        diff = sb("diff", [P, TILES])
        spread = sb("spread", [P, TILES])
        var_eps = sb("var_eps", [P, TILES])
        minus_half = sb("minus_half", [P, TILES])
        rstd = sb("rstd", [P, TILES])
        z_hi = sb("z_hi", [P, KT, D], F32R)
        z_lo = sb("z_lo", [P, KT, D], F32R)
        with ExitStack() as first:
            y_hi = sb("y_hi", [P, KT, D], F32R, first)
            y_lo = sb("y_lo", [P, KT, D], F32R, first)
        res_h = sb("res_h", [P, HALVES, BLOCK])
        res_x = sb("res_x", [P, HALVES, BLOCK])
        norm = sb("norm", [P, TILES, D])

        acc = ctx.enter_context(nc.psum_tensor("acc", [P, HALVES, BLOCK], F32))
        rows = [ctx.enter_context(nc.psum_tensor(f"rows{i}", [P, TILES, D], F32)) for i in range(2)]

        raw_landed = [sem(f"raw_landed{i}") for i in range(RING)]
        const_landed = sem("const_landed")
        w_landed = sem("w_landed")
        feat_landed = sem("feat_landed")
        res_landed = sem("res_landed")
        h_stored = sem("h_stored")
        out_stored = sem("out_stored")
        hi_ready = sem("hi_ready")
        lo_ready = sem("lo_ready")
        chunk_used = sem("chunk_used")
        w_hi_ready = sem("w_hi_ready")
        w_lo_ready = sem("w_lo_ready")
        feat_hi_ready = sem("feat_hi_ready")
        feat_lo_ready = sem("feat_lo_ready")
        feat_used = sem("feat_used")
        y_hi_ready = sem("y_hi_ready")
        y_lo_ready = sem("y_lo_ready")
        z_hi_ready = sem("z_hi_ready")
        z_lo_ready = sem("z_lo_ready")
        half_done = sem("half_done")
        act_ready = sem("act_ready")
        sum_ready = sem("sum_ready")
        resid_ready = sem("resid_ready")
        turned = sem("turned")
        stats_ready = sem("stats_ready")
        pair_ready = sem("pair_ready")
        mean_ready = sem("mean_ready")
        eps_ready = sem("eps_ready")
        minus_half_ready = sem("minus_half_ready")
        rstd_ready = sem("rstd_ready")
        norm_ready = sem("norm_ready")

        def chunks_before(layer, b):
            return BLOCKS + layer * BLOCKS * CHUNKS + b * CHUNKS

        def blocks_before(layer, b):
            return layer * BLOCKS + b

        def self_split(layer, b):
            return 2 * b if layer == 0 else 2 * BLOCKS + b

        def h_split(b):
            return 2 * b + 1

        block = ctx.enter_context(nc.Block())

        @block.sync
        def _(sp):
            def load_chunk(src, slot, n):
                if not isinstance(n, int) or n >= RING:
                    sp.wait_ge(lo_ready, n - RING + 1)
                sp.dma_start(raw[slot][:], src).then_inc(raw_landed[slot], 16)

            def load_weights(w, part, n):
                if n:
                    sp.wait_ge(w_lo_ready, n)
                sp.dma_start(w_raw[:], w[part]).then_inc(w_landed, 16)

            def load_feats(layer, b, first):
                if layer == 0 and not first:
                    sp.wait_ge(feat_lo_ready, self_split(0, b) - 1)
                if layer == 1 and first:
                    sp.wait_ge(feat_lo_ready, self_split(1, 0) - 1)
                    sp.wait_ge(h_stored, 16 * (BLOCKS - 1))
                if layer == 1 and not first:
                    sp.wait_ge(feat_lo_ready, self_split(1, b))
                src = x_t if layer == 0 else h_t
                sp.dma_start(feat_raw[:], src[b]).then_inc(feat_landed, 16)

            def store_h(b):
                sp.wait_ge(act_ready, HALVES * (b + 1))
                sp.dma_start(h_t[b], act_t[:]).then_inc(h_stored, 16)

            def load_residuals(b):
                sp.dma_start(res_h[:], h_t[b]).then_inc(res_landed, 16)
                sp.dma_start(res_x[:], x_t[b]).then_inc(res_landed, 16)

            def store_rows(b):
                sp.wait_ge(norm_ready, TILES * (b + 1))
                sp.dma_start(out[b], norm[:]).then_inc(out_stored, 16)

            def load_block(layer, b, first=False):
                for c in range(CHUNKS):
                    load_chunk(adj_t[b, c], c % RING,
                               chunks_before(layer, b) + c)
                    if c == 0:
                        load_feats(layer, b, first)
                    if c == STORE_AT and layer == 0 and not first:
                        store_h(b - 1)
                    if c == STORE_AT and layer == 1 and first:
                        store_h(BLOCKS - 1)
                        sp.wait_ge(h_stored, 16 * BLOCKS)
                        sp.wait_ge(chunk_used, chunks_before(1, 0))
                        load_residuals(0)
                    if c == STORE_AT and layer == 1 and not first:
                        sp.wait_ge(resid_ready, b)
                        load_residuals(b)
                    if c == CHUNKS - 3 and layer == 1 and not first:
                        store_rows(b - 1)

            load_weights(w1, 1, 0)
            for b in range(BLOCKS):
                load_chunk(x_t[b], b % RING, b)
                if b == 1:
                    load_weights(w1, 0, 1)
                if b == 3:
                    sp.dma_start(bias1[:], b1).then_inc(const_landed, 16)
                    sp.dma_start(bias2[:], b2).then_inc(const_landed, 16)
                    sp.dma_start(identity[:], ident).then_inc(const_landed, 16)
            load_weights(w2, 1, 2)
            load_block(0, 0, first=True)
            with sp.Fori(1, BLOCKS) as b:
                load_block(0, b)
            load_weights(w2, 0, 3)
            load_block(1, 0, first=True)
            with sp.Fori(1, BLOCKS) as b:
                load_block(1, b)
            store_rows(BLOCKS - 1)
            sp.wait_ge(out_stored, 16 * BLOCKS)

        @block.scalar
        def _(act):
            def chunk_high(c, n):
                act.wait_ge(raw_landed[c % RING], fills(n, c))
                if not isinstance(n, int) or n >= RING:
                    act.wait_ge(chunk_used, n - RING + 1)
                nc.scalar.activation(chunk_hi[c % RING][:], raw[c % RING][:],
                                     ACT.Copy).then_inc(hi_ready, 1)

            def fills(n, c):
                return n // RING * 16 + 16 if isinstance(n, int) else (n - c) * (16 // RING) + c // RING * 16 + 16

            def weights_high(n):
                act.wait_ge(w_landed, 16 * (n + 1))
                if n == 2:
                    act.wait_ge(chunk_used, BLOCKS)
                if n == 3:
                    act.wait_ge(feat_used, self_split(0, BLOCKS - 1) + 1)
                nc.scalar.activation(w_hi[n % 2][:], w_raw[:], ACT.Copy).then_inc(w_hi_ready, 1)

            def y_high(b):
                act.wait_ge(chunk_used, b + 1)
                nc.scalar.activation(y_hi[:, b * TILES:(b + 1) * TILES, :], rows[b % 2][:],
                                     ACT.Copy).then_inc(y_hi_ready, 1)

            def z_high(b):
                act.wait_ge(feat_used, h_split(b) + 1)
                nc.scalar.activation(z_hi[:, bass.ds(b * TILES, TILES), :], rows[0][:],
                                     ACT.Copy).then_inc(z_hi_ready, 1)

            def feat_high(src, n):
                if not isinstance(n, int) or n:
                    act.wait_ge(feat_used, n)
                nc.scalar.activation(feat_hi[:], src, ACT.Copy).then_inc(feat_hi_ready, 1)

            def self_high(layer, b):
                act.wait_ge(feat_landed, 16 * (blocks_before(layer, b) + 1))
                feat_high(feat_raw[:], self_split(layer, b))

            def evacuate(layer, b):
                bias = (bias1, bias2)[layer]
                for half in range(HALVES):
                    if half == 0:
                        act.wait_ge(half_done, blocks_before(layer, b) + 1)
                    else:
                        act.wait_ge(chunk_used, chunks_before(layer, b) + CHUNKS)
                    nc.scalar.activation(act_t[:, half, :], acc[:, half, :], ACT.Relu,
                                         bias=bias[:, half:half + 1]).then_inc(act_ready, 1)

            def h_high(b):
                act.wait_ge(act_ready, HALVES * (b + 1))
                feat_high(act_t[:], h_split(b))

            def split_block(layer, b, first=False):
                of_h = (b - 1 if layer == 0 else BLOCKS - 1) if first == (layer == 1) else None
                for c in range(CHUNKS):
                    if layer == 0 and first and c < RING:
                        y_high(BLOCKS - RING + c)
                    chunk_high(c, chunks_before(layer, b) + c)
                    if layer == 0 and first and c == RING:
                        weights_high(2)
                    if of_h is not None and c == EVAC_AT:
                        evacuate(0, of_h)
                    if of_h is not None and c == EVAC_AT + 1:
                        h_high(of_h)
                    if of_h is not None and c == ROWS_AT + RING + 1:
                        z_high(of_h)
                    if layer == 1 and not first and c == EVAC_AT:
                        evacuate(1, b - 1)
                    if layer == 1 and first and c == SELF_AT - 2:
                        weights_high(3)
                    if c == SELF_AT - 1:
                        self_high(layer, b)
                act_t_free(layer, b, first)

            def act_t_free(layer, b, first):
                if layer == 0 and not first:
                    act.wait_ge(h_stored, 16 * b)
                if layer == 1 and first:
                    act.wait_ge(h_stored, 16 * BLOCKS)
                if layer == 1 and not first:
                    act.wait_ge(turned, b)

            weights_high(0)
            for b in range(BLOCKS):
                if b >= RING:
                    y_high(b - RING)
                chunk_high(b, b)
                if b == 2:
                    weights_high(1)
            act.wait_ge(const_landed, 48)
            split_block(0, 0, first=True)
            with act.Fori(1, BLOCKS) as b:
                split_block(0, b)
            split_block(1, 0, first=True)
            with act.Fori(1, BLOCKS) as b:
                split_block(1, b)
            evacuate(1, BLOCKS - 1)

        @block.vector
        def _(dve):
            def low(out_lo, src, hi):
                return nc.vector.tensor_tensor(out=out_lo, in0=src, in1=hi.bitcast(F32),
                                               op=ALU.subtract)

            def chunk_low(c, n):
                dve.wait_ge(hi_ready, n + 1)
                low(chunk_lo[c % RING][:], raw[c % RING][:], chunk_hi[c % RING][:]).then_inc(lo_ready, 1)

            def weights_low(n):
                dve.wait_ge(w_hi_ready, n + 1)
                low(w_lo[n % 2][:], w_raw[:], w_hi[n % 2][:]).then_inc(w_lo_ready, 1)

            def y_low(b):
                dve.wait_ge(y_hi_ready, b + 1)
                at = slice(b * TILES, (b + 1) * TILES)
                low(y_lo[:, at, :], rows[b % 2][:], y_hi[:, at, :]).then_inc(y_lo_ready, 1)

            def z_low(b):
                dve.wait_ge(z_hi_ready, b + 1)
                at = bass.ds(b * TILES, TILES)
                low(z_lo[:, at, :], rows[0][:], z_hi[:, at, :]).then_inc(z_lo_ready, 1)

            def feat_low(src, n):
                dve.wait_ge(feat_hi_ready, n + 1)
                low(feat_lo[:], src, feat_hi[:]).then_inc(feat_lo_ready, 1)

            def residual_h(b):
                dve.wait_ge(res_landed, 2 * 16 * (b + 1))
                dve.wait_ge(act_ready, HALVES * (blocks_before(1, b) + 1))
                nc.vector.tensor_tensor(out=act_t[:], in0=act_t[:], in1=res_h[:],
                                        op=ALU.add).then_inc(sum_ready, 1)

            def residual_x(b):
                dve.wait_ge(sum_ready, b + 1)
                nc.vector.scalar_tensor_tensor(out=act_t[:], in0=act_t[:], scalar=0.0, in1=res_x[:],
                                               op0=ALU.max, op1=ALU.add).then_inc(resid_ready, 1)

            def normalize(b):
                dve.wait_ge(turned, b + 1)
                for j in range(TILES):
                    nc.vector.bn_stats(stats[:, j, :], rows[1][:, j, :]).then_inc(stats_ready, 1)
                dve.wait_ge(stats_ready, TILES * (b + 1))
                nc.vector.tensor_tensor(out=mean[:], in0=stats[:, :, 1], in1=stats[:, :, 4],
                                        op=ALU.add).then_inc(pair_ready, 1)
                nc.vector.tensor_tensor(out=diff[:], in0=stats[:, :, 1], in1=stats[:, :, 4],
                                        op=ALU.subtract).then_inc(pair_ready, 1)
                nc.vector.scalar_tensor_tensor(out=spread[:], in0=stats[:, :, 2], scalar=EPS * D,
                                               in1=stats[:, :, 5], op0=ALU.add,
                                               op1=ALU.add).then_inc(pair_ready, 1)
                dve.wait_ge(pair_ready, 3 * (b + 1))
                nc.vector.tensor_scalar(mean[:], mean[:], 0.5, None, ALU.mult).then_inc(mean_ready, 1)
                nc.vector.scalar_tensor_tensor(out=diff[:], in0=diff[:], scalar=0.25, in1=diff[:],
                                               op0=ALU.mult, op1=ALU.mult).then_inc(mean_ready, 1)
                dve.wait_ge(mean_ready, 2 * (b + 1))
                nc.vector.scalar_tensor_tensor(out=var_eps[:], in0=spread[:], scalar=1.0 / D,
                                               in1=diff[:], op0=ALU.mult,
                                               op1=ALU.add).then_inc(eps_ready, 1)
                dve.wait_ge(rstd_ready, b + 1)
                for j in range(TILES):
                    nc.vector.tensor_scalar(norm[:, j, :], rows[1][:, j, :], mean[:, j:j + 1],
                                            rstd[:, j:j + 1], ALU.subtract, ALU.mult)\
                        .then_inc(norm_ready, 1)

            def split_block(layer, b, first=False):
                of_h = (b - 1 if layer == 0 else BLOCKS - 1) if first == (layer == 1) else None
                for c in range(CHUNKS):
                    if layer == 0 and first and c < RING:
                        y_low(BLOCKS - RING + c)
                    chunk_low(c, chunks_before(layer, b) + c)
                    if layer == 0 and first and c == RING:
                        weights_low(2)
                    if of_h is not None and c == EVAC_AT + 1:
                        feat_low(act_t[:], h_split(of_h))
                    if of_h is not None and c == ROWS_AT + RING + 1:
                        z_low(of_h)
                    if layer == 1 and not first and c == EVAC_AT + 1:
                        residual_h(b - 1)
                    if layer == 1 and not first and c == EVAC_AT + 2:
                        residual_x(b - 1)
                    if layer == 1 and not first and c == ROWS_AT + RING + 1:
                        normalize(b - 1)
                    if layer == 1 and first and c == SELF_AT - 2:
                        weights_low(3)
                    if c == SELF_AT - 1:
                        feat_low(feat_raw[:], self_split(layer, b))
                if layer == 1 and not first:
                    dve.wait_ge(out_stored, 16 * b)

            weights_low(0)
            for b in range(BLOCKS):
                if b >= RING:
                    y_low(b - RING)
                chunk_low(b, b)
                if b == 2:
                    weights_low(1)
            split_block(0, 0, first=True)
            with dve.Fori(1, BLOCKS) as b:
                split_block(0, b)
            split_block(1, 0, first=True)
            with dve.Fori(1, BLOCKS) as b:
                split_block(1, b)
            residual_h(BLOCKS - 1)
            residual_x(BLOCKS - 1)
            normalize(BLOCKS - 1)

        @block.gpsimd
        def _(pool):
            nc.gpsimd.memset(minus_half[:], -0.5).then_inc(minus_half_ready, 1)
            pool.wait_ge(minus_half_ready, 1)
            with pool.Fori(0, BLOCKS) as b:
                pool.wait_ge(eps_ready, b + 1)
                nc.gpsimd.tensor_tensor(out=rstd[:], in0=var_eps[:], in1=minus_half[:],
                                        op=ALU.pow).then_inc(rstd_ready, 1)

        @block.tensor
        def _(pe):
            def product(dst, stationary, moving, start, stop):
                (sh, sl), (mh, ml) = stationary, moving
                nc.tensor.matmul(dst, sh, mh, start=start, stop=False)
                nc.tensor.matmul(dst, sh, ml, start=False, stop=False)
                return nc.tensor.matmul(dst, sl, mh, start=False, stop=stop)

            def row_products(dst, hi, lo):
                for j in range(TILES):
                    n = slice(j * P, (j + 1) * P)
                    for f in range(HALVES):
                        last = product(dst[:, j, :], (hi[:, f, n], lo[:, f, n]),
                                       (w_hi[0][:, f, :], w_lo[0][:, f, :]),
                                       f == 0, f == HALVES - 1)
                return last

            def make_y(b):
                pe.wait_ge(lo_ready, b + 1)
                if b >= 2:
                    pe.wait_ge(y_lo_ready, b - 1)
                row_products(rows[b % 2], chunk_hi[b % RING], chunk_lo[b % RING])\
                    .then_inc(chunk_used, 1)

            def make_z(b):
                pe.wait_ge(feat_lo_ready, h_split(b) + 1)
                row_products(rows[0], feat_hi, feat_lo).then_inc(feat_used, 1)

            def self_term(layer, b):
                pe.wait_ge(feat_lo_ready, self_split(layer, b) + 1)
                for half in range(HALVES):
                    g = slice(half * P, (half + 1) * P)
                    for f in range(HALVES):
                        last = product(acc[:, half, :], (w_hi[1][:, f, g], w_lo[1][:, f, g]),
                                       (feat_hi[:, f, :], feat_lo[:, f, :]), False, False)
                last.then_inc(feat_used, 1)

            def aggregate(layer, b, c):
                v_hi, v_lo = ((y_hi, y_lo), (z_hi, z_lo))[layer]
                pe.wait_ge(lo_ready, chunks_before(layer, b) + c + 1)
                for half in range(HALVES):
                    if c == 0 and not (layer == 0 and isinstance(b, int)):
                        pe.wait_ge(act_ready, HALVES * (blocks_before(layer, b) - 1) + half + 1)
                    g = slice(half * P, (half + 1) * P)
                    for j in range(CK):
                        k = c * CK + j
                        last = product(acc[:, half, :], (v_hi[:, k, g], v_lo[:, k, g]),
                                       (chunk_hi[c % RING][:, j, :], chunk_lo[c % RING][:, j, :]),
                                       k == 0, k == KT - 1)
                    if c == CHUNKS - 1 and half == 0:
                        last.then_inc(half_done, 1)
                last.then_inc(chunk_used, 1)

            def turn(b):
                pe.wait_ge(resid_ready, b + 1)
                for j in range(TILES):
                    for half in range(HALVES):
                        last = nc.tensor.transpose(rows[1][:, j, half * P:(half + 1) * P],
                                                   act_t[:, half, j * P:(j + 1) * P], identity[:])
                last.then_inc(turned, 1)

            def block_products(layer, b, first=False):
                of_h = (b - 1 if layer == 0 else BLOCKS - 1) if first == (layer == 1) else None
                for c in range(CHUNKS):
                    if first and layer == 0 and c % CPB == 0:
                        pe.wait_ge(y_lo_ready, c // CPB + 1)
                    if first and layer == 1 and c == 0:
                        pe.wait_ge(z_lo_ready, BLOCKS - 1)
                    if first and layer == 1 and c == CHUNKS - CPB:
                        pe.wait_ge(z_lo_ready, BLOCKS)
                    aggregate(layer, b, c)
                    if c == ROWS_AT and of_h is not None:
                        if layer == 0:
                            pe.wait_ge(w_lo_ready, 3)
                        make_z(of_h)
                    if c == ROWS_AT and layer == 1 and not first:
                        turn(b - 1)
                    if c == SELF_AT:
                        if first:
                            pe.wait_ge(w_lo_ready, 2 * (layer + 1))
                        self_term(layer, b)
                if layer == 0 and first:
                    pe.wait_ge(y_lo_ready, BLOCKS)
                if layer == 0 and not first:
                    pe.wait_ge(z_lo_ready, b)
                if layer == 1 and not first:
                    pe.wait_ge(norm_ready, TILES * b)

            pe.wait_ge(w_lo_ready, 1)
            for b in range(BLOCKS):
                make_y(b)
            block_products(0, 0, first=True)
            with pe.Fori(1, BLOCKS) as b:
                block_products(0, b)
            block_products(1, 0, first=True)
            pe.wait_ge(const_landed, 48)
            with pe.Fori(1, BLOCKS) as b:
                block_products(1, b)
            turn(BLOCKS - 1)


def kernel(x, adj, L0_gnn_W1, L0_gnn_b1, L0_gnn_W2, L0_gnn_b2):
    import numpy as np
    import concourse.bacc as bacc
    from concourse.bass_utils import run_bass_kernel_spmd

    n, d = x.shape
    blocks, kt, halves = n // BLOCK, n // P, d // P
    ready = np.ascontiguousarray

    def weights(w):
        return ready(np.asarray(w).reshape(2, halves, P, d).transpose(0, 2, 1, 3))

    arrays = {
        "adj_t": ready(np.asarray(adj).reshape(blocks, BLOCK, kt // CK, CK, P)
                       .transpose(0, 2, 4, 3, 1)),
        "x_t": ready(np.asarray(x).reshape(blocks, BLOCK, halves, P).transpose(0, 3, 2, 1)),
        "w1": weights(L0_gnn_W1),
        "w2": weights(L0_gnn_W2),
        "b1": ready(np.asarray(L0_gnn_b1).reshape(halves, P).T),
        "b2": ready(np.asarray(L0_gnn_b2).reshape(halves, P).T),
        "ident": np.eye(P, dtype=np.float32),
    }
    nc = bacc.Bacc("TRN2", target_bir_lowering=False, num_devices=1)
    ins = {name: nc.dram_tensor(name, a.shape, F32, kind="ExternalInput").ap()
           for name, a in arrays.items()}
    h_t = nc.dram_tensor("h_t", arrays["x_t"].shape, F32).ap()
    out = nc.dram_tensor("out", (blocks, P, BLOCK // P, d), F32, kind="ExternalOutput").ap()
    graph_resnorm_kernel(nc, h_t=h_t, out=out, **ins)
    got = run_bass_kernel_spmd(nc, [arrays], core_ids=[0]).results[0]["out"]
    return ready(got.transpose(0, 2, 1, 3).reshape(n, d))
```

```python
from contextlib import ExitStack

import concourse.bass as bass
from concourse import mybir


F32 = mybir.dt.float32
F32R = mybir.dt.float32r
ALU = mybir.AluOpType
ACT = mybir.ActivationFunctionType

P = 128
BLOCK = 512
CK = 2
EPS = 1e-5


def graph_resnorm_kernel(nc, adj_t, x_t, w1, w2, b1, b2, ident, h_t, out):
    BLOCKS, CHUNKS = adj_t.shape[:2]
    KT = CHUNKS * CK
    HALVES = x_t.shape[2]
    D = HALVES * P
    TILES = BLOCK // P
    PAIR = TILES // 2
    RING = 4
    assert HALVES * BLOCK == CK * BLOCK and CHUNKS % RING == 0 and BLOCKS % RING == 0
    CPB = CHUNKS // BLOCKS
    HEAD, REST = slice(0, PAIR * P), slice(PAIR * P, BLOCK)
    EVAC_AT = RING - 2
    ROWS_AT = 4
    SELF_AT = 11
    ROWS_READY_AT = ROWS_AT + RING + 1
    NORM_AT = ROWS_READY_AT + 2
    STORE_AT = 9

    with ExitStack() as ctx:
        def sb(name, shape, dt=F32, where=ctx):
            return where.enter_context(nc.sbuf_tensor(name, shape, dt))

        def sem(name):
            return ctx.enter_context(nc.semaphore(name))

        raw = [sb(f"raw{i}", [P, CK, BLOCK]) for i in range(RING)]
        chunk_hi = [sb(f"chunk_hi{i}", [P, CK, BLOCK], F32R) for i in range(RING)]
        chunk_lo = [sb(f"chunk_lo{i}", [P, CK, BLOCK], F32R) for i in range(RING)]
        w_raw = sb("w_raw", [P, HALVES, D])
        w_hi = [sb(f"w_hi{i}", [P, HALVES, D], F32R) for i in range(2)]
        w_lo = [sb(f"w_lo{i}", [P, HALVES, D], F32R) for i in range(2)]
        feat_raw = sb("feat_raw", [P, HALVES, BLOCK])
        feat_hi = sb("feat_hi", [P, HALVES, BLOCK], F32R)
        feat_lo = sb("feat_lo", [P, HALVES, BLOCK], F32R)
        act_t = sb("act_t", [P, HALVES, BLOCK])
        bias1 = sb("bias1", [P, HALVES])
        bias2 = sb("bias2", [P, HALVES])
        identity = sb("identity", [P, P])
        stats = sb("stats", [P, TILES, 6])
        mean = sb("mean", [P, TILES])
        diff = sb("diff", [P, TILES])
        spread = sb("spread", [P, TILES])
        var_eps = sb("var_eps", [P, TILES])
        minus_half = sb("minus_half", [P, TILES])
        rstd = sb("rstd", [P, TILES])
        shift = sb("shift", [P, TILES])
        z_hi = sb("z_hi", [P, KT, D], F32R)
        z_lo = sb("z_lo", [P, KT, D], F32R)
        with ExitStack() as first:
            y_hi = sb("y_hi", [P, KT, D], F32R, first)
            y_lo = sb("y_lo", [P, KT, D], F32R, first)
        res_h = sb("res_h", [P, HALVES, BLOCK])
        res_x = sb("res_x", [P, HALVES, BLOCK])
        norm = [sb(f"norm{pair}", [P, PAIR, D]) for pair in range(2)]

        acc = ctx.enter_context(nc.psum_tensor("acc", [P, HALVES, BLOCK], F32))
        rows = [ctx.enter_context(nc.psum_tensor(f"rows{i}", [P, TILES, D], F32)) for i in range(2)]

        raw_landed = [sem(f"raw_landed{i}") for i in range(RING)]
        head_landed = sem("head_landed")
        head_hi_ready = sem("head_hi_ready")
        head_lo_ready = sem("head_lo_ready")
        const_landed = sem("const_landed")
        w_landed = sem("w_landed")
        feat_landed = sem("feat_landed")
        res_landed = sem("res_landed")
        h_stored = sem("h_stored")
        out_stored = [sem(f"out_stored{pair}") for pair in range(2)]
        hi_ready = sem("hi_ready")
        lo_ready = sem("lo_ready")
        chunk_used = sem("chunk_used")
        w_hi_ready = sem("w_hi_ready")
        w_lo_ready = sem("w_lo_ready")
        feat_hi_ready = sem("feat_hi_ready")
        feat_lo_ready = sem("feat_lo_ready")
        feat_used = sem("feat_used")
        y_hi_ready = sem("y_hi_ready")
        y_lo_ready = sem("y_lo_ready")
        z_hi_ready = sem("z_hi_ready")
        z_lo_ready = sem("z_lo_ready")
        half_done = sem("half_done")
        act_ready = sem("act_ready")
        sum_ready = sem("sum_ready")
        resid_ready = sem("resid_ready")
        turned = sem("turned")
        stats_ready = sem("stats_ready")
        pair_ready = sem("pair_ready")
        mean_ready = sem("mean_ready")
        eps_ready = sem("eps_ready")
        minus_half_ready = sem("minus_half_ready")
        rstd_ready = sem("rstd_ready")
        shift_ready = sem("shift_ready")
        norm_ready = [sem(f"norm_ready{pair}") for pair in range(2)]

        def chunks_before(layer, b):
            return BLOCKS + layer * BLOCKS * CHUNKS + b * CHUNKS

        def blocks_before(layer, b):
            return layer * BLOCKS + b

        def self_split(layer, b):
            return 2 * b if layer == 0 else 2 * BLOCKS + b

        def h_split(b):
            return 2 * b + 1

        block = ctx.enter_context(nc.Block())

        @block.sync
        def _(sp):
            def load_chunk(src, slot, n):
                if not isinstance(n, int) or n >= RING:
                    sp.wait_ge(lo_ready, n - RING + 1)
                sp.dma_start(raw[slot][:], src).then_inc(raw_landed[slot], 16)

            def load_weights(w, part, n):
                if n:
                    sp.wait_ge(w_lo_ready, n)
                sp.dma_start(w_raw[:], w[part]).then_inc(w_landed, 16)

            def load_feats(layer, b, first):
                if layer == 0 and not first:
                    sp.wait_ge(feat_lo_ready, self_split(0, b) - 1)
                if layer == 1 and first:
                    sp.wait_ge(feat_lo_ready, self_split(1, 0) - 1)
                    sp.wait_ge(h_stored, 16 * (BLOCKS - 1))
                if layer == 1 and not first:
                    sp.wait_ge(feat_lo_ready, self_split(1, b))
                src = x_t if layer == 0 else h_t
                sp.dma_start(feat_raw[:], src[b]).then_inc(feat_landed, 16)

            def store_h(b):
                sp.wait_ge(act_ready, HALVES * (b + 1))
                sp.dma_start(h_t[b], act_t[:]).then_inc(h_stored, 16)

            def load_residuals(b):
                sp.dma_start(res_h[:], h_t[b]).then_inc(res_landed, 16)
                sp.dma_start(res_x[:], x_t[b]).then_inc(res_landed, 16)

            def store_rows(b):
                for pair in range(2):
                    sp.wait_ge(norm_ready[pair], b + 1)
                    sp.dma_start(out[b, pair], norm[pair][:]).then_inc(out_stored[pair], 16)

            def load_block(layer, b, first=False):
                for c in range(CHUNKS):
                    load_chunk(adj_t[b, c], c % RING,
                               chunks_before(layer, b) + c)
                    if c == 0:
                        load_feats(layer, b, first)
                    if c == STORE_AT and layer == 0 and not first:
                        store_h(b - 1)
                    if c == STORE_AT and layer == 1 and first:
                        store_h(BLOCKS - 1)
                        sp.wait_ge(h_stored, 16 * BLOCKS)
                        sp.wait_ge(chunk_used, chunks_before(1, 0))
                        load_residuals(0)
                    if c == STORE_AT and layer == 1 and not first:
                        sp.wait_ge(resid_ready, HALVES * b)
                        load_residuals(b)
                    if c == CHUNKS - 3 and layer == 1 and not first:
                        store_rows(b - 1)

            sp.dma_start(raw[0][:, :, HEAD], x_t[0, :, :, HEAD]).then_inc(head_landed, 16)
            load_weights(w1, 1, 0)
            sp.dma_start(raw[0][:, :, REST], x_t[0, :, :, REST]).then_inc(raw_landed[0], 16)
            for b in range(1, BLOCKS):
                load_chunk(x_t[b], b % RING, b)
                if b == 3:
                    load_weights(w1, 0, 1)
                    sp.dma_start(bias1[:], b1).then_inc(const_landed, 16)
                    sp.dma_start(bias2[:], b2).then_inc(const_landed, 16)
                    sp.dma_start(identity[:], ident).then_inc(const_landed, 16)
            load_weights(w2, 1, 2)
            load_block(0, 0, first=True)
            with sp.Fori(1, BLOCKS) as b:
                load_block(0, b)
            load_weights(w2, 0, 3)
            load_block(1, 0, first=True)
            with sp.Fori(1, BLOCKS) as b:
                load_block(1, b)
            store_rows(BLOCKS - 1)
            for pair in range(2):
                sp.wait_ge(out_stored[pair], 16 * BLOCKS)

        @block.scalar
        def _(act):
            def chunk_high(c, n):
                act.wait_ge(raw_landed[c % RING], fills(n, c))
                if not isinstance(n, int) or n >= RING:
                    act.wait_ge(chunk_used, n - RING + 1)
                nc.scalar.activation(chunk_hi[c % RING][:], raw[c % RING][:],
                                     ACT.Copy).then_inc(hi_ready, 1)

            def fills(n, c):
                if isinstance(n, int):
                    return 16 * (n // RING + 1)
                return (n - c) * (16 // RING) + 16 * (c // RING + 1)

            def weights_high(n):
                act.wait_ge(w_landed, 16 * (n + 1))
                if n == 2:
                    act.wait_ge(chunk_used, BLOCKS)
                if n == 3:
                    act.wait_ge(feat_used, self_split(0, BLOCKS - 1) + 1)
                nc.scalar.activation(w_hi[n % 2][:], w_raw[:], ACT.Copy).then_inc(w_hi_ready, 1)

            def y_high(b):
                act.wait_ge(chunk_used, b + 1)
                nc.scalar.activation(y_hi[:, b * TILES:(b + 1) * TILES, :], rows[b % 2][:],
                                     ACT.Copy).then_inc(y_hi_ready, 1)

            def z_high(b):
                act.wait_ge(feat_used, h_split(b) + 1)
                nc.scalar.activation(z_hi[:, bass.ds(b * TILES, TILES), :], rows[0][:],
                                     ACT.Copy).then_inc(z_hi_ready, 1)

            def feat_high(src, n):
                if not isinstance(n, int) or n:
                    act.wait_ge(feat_used, n)
                nc.scalar.activation(feat_hi[:], src, ACT.Copy).then_inc(feat_hi_ready, 1)

            def self_high(layer, b):
                act.wait_ge(feat_landed, 16 * (blocks_before(layer, b) + 1))
                feat_high(feat_raw[:], self_split(layer, b))

            def evacuate(layer, b):
                bias = (bias1, bias2)[layer]
                for half in range(HALVES):
                    if half == 0:
                        act.wait_ge(half_done, blocks_before(layer, b) + 1)
                    else:
                        act.wait_ge(chunk_used, chunks_before(layer, b) + CHUNKS)
                    nc.scalar.activation(act_t[:, half, :], acc[:, half, :], ACT.Relu,
                                         bias=bias[:, half:half + 1]).then_inc(act_ready, 1)

            def h_high(b):
                act.wait_ge(act_ready, HALVES * (b + 1))
                feat_high(act_t[:], h_split(b))

            def normalize(b):
                act.wait_ge(shift_ready, b + 1)
                for j in range(PAIR):
                    at = slice(PAIR + j, PAIR + j + 1)
                    last = nc.scalar.activation(norm[1][:, j, :], rows[1][:, PAIR + j, :],
                                                ACT.Identity, bias=shift[:, at], scale=rstd[:, at])
                last.then_inc(norm_ready[1], 1)

            def split_block(layer, b, first=False):
                of_h = (b - 1 if layer == 0 else BLOCKS - 1) if first == (layer == 1) else None
                for c in range(CHUNKS):
                    if layer == 0 and first and c < RING:
                        y_high(BLOCKS - RING + c)
                    chunk_high(c, chunks_before(layer, b) + c)
                    if layer == 0 and first and c == RING:
                        weights_high(2)
                    if of_h is not None and c == EVAC_AT:
                        evacuate(0, of_h)
                    if of_h is not None and c == EVAC_AT + 1:
                        h_high(of_h)
                    if of_h is not None and c == ROWS_READY_AT:
                        z_high(of_h)
                    if layer == 1 and not first and c == EVAC_AT:
                        evacuate(1, b - 1)
                    if layer == 1 and not first and c == NORM_AT:
                        normalize(b - 1)
                    if layer == 1 and first and c == SELF_AT - 2:
                        weights_high(3)
                    if c == SELF_AT - 1:
                        self_high(layer, b)
                act_t_free(layer, b, first)

            def act_t_free(layer, b, first):
                if layer == 0 and not first:
                    act.wait_ge(h_stored, 16 * b)
                if layer == 1 and first:
                    act.wait_ge(h_stored, 16 * BLOCKS)
                if layer == 1 and not first:
                    act.wait_ge(turned, 2 * b)
                    act.wait_ge(out_stored[1], 16 * b)

            act.wait_ge(head_landed, 16)
            nc.scalar.activation(chunk_hi[0][:, :, HEAD], raw[0][:, :, HEAD],
                                 ACT.Copy).then_inc(head_hi_ready, 1)
            weights_high(0)
            act.wait_ge(raw_landed[0], 16)
            nc.scalar.activation(chunk_hi[0][:, :, REST], raw[0][:, :, REST],
                                 ACT.Copy).then_inc(hi_ready, 1)
            for b in range(1, BLOCKS):
                if b >= RING:
                    y_high(b - RING)
                chunk_high(b, b)
                if b == RING:
                    weights_high(1)
            act.wait_ge(const_landed, 48)
            split_block(0, 0, first=True)
            with act.Fori(1, BLOCKS) as b:
                split_block(0, b)
            split_block(1, 0, first=True)
            with act.Fori(1, BLOCKS) as b:
                split_block(1, b)
            evacuate(1, BLOCKS - 1)
            normalize(BLOCKS - 1)

        @block.vector
        def _(dve):
            def low(out_lo, src, hi):
                return nc.vector.tensor_tensor(out=out_lo, in0=src, in1=hi.bitcast(F32),
                                               op=ALU.subtract)

            def chunk_low(c, n):
                dve.wait_ge(hi_ready, n + 1)
                low(chunk_lo[c % RING][:], raw[c % RING][:], chunk_hi[c % RING][:]).then_inc(lo_ready, 1)

            def weights_low(n):
                dve.wait_ge(w_hi_ready, n + 1)
                low(w_lo[n % 2][:], w_raw[:], w_hi[n % 2][:]).then_inc(w_lo_ready, 1)

            def y_low(b):
                dve.wait_ge(y_hi_ready, b + 1)
                at = slice(b * TILES, (b + 1) * TILES)
                low(y_lo[:, at, :], rows[b % 2][:], y_hi[:, at, :]).then_inc(y_lo_ready, 1)

            def z_low(b):
                dve.wait_ge(z_hi_ready, b + 1)
                at = bass.ds(b * TILES, TILES)
                low(z_lo[:, at, :], rows[0][:], z_hi[:, at, :]).then_inc(z_lo_ready, 1)

            def feat_low(src, n):
                dve.wait_ge(feat_hi_ready, n + 1)
                low(feat_lo[:], src, feat_hi[:]).then_inc(feat_lo_ready, 1)

            def residuals(b):
                dve.wait_ge(res_landed, 2 * 16 * (b + 1))
                for half in range(HALVES):
                    dve.wait_ge(act_ready, HALVES * blocks_before(1, b) + half + 1)
                    nc.vector.tensor_tensor(out=act_t[:, half, :], in0=act_t[:, half, :],
                                            in1=res_h[:, half, :], op=ALU.add).then_inc(sum_ready, 1)
                    dve.wait_ge(sum_ready, HALVES * b + half + 1)
                    nc.vector.scalar_tensor_tensor(out=act_t[:, half, :], in0=act_t[:, half, :],
                                                   scalar=0.0, in1=res_x[:, half, :], op0=ALU.max,
                                                   op1=ALU.add).then_inc(resid_ready, 1)

            def normalize(b):
                for j in range(TILES):
                    if j % PAIR == 0:
                        dve.wait_ge(turned, 2 * b + j // PAIR + 1)
                    nc.vector.bn_stats(stats[:, j, :], rows[1][:, j, :]).then_inc(stats_ready, 1)
                dve.wait_ge(stats_ready, TILES * (b + 1))
                nc.vector.tensor_tensor(out=mean[:], in0=stats[:, :, 1], in1=stats[:, :, 4],
                                        op=ALU.add).then_inc(pair_ready, 1)
                nc.vector.tensor_tensor(out=diff[:], in0=stats[:, :, 1], in1=stats[:, :, 4],
                                        op=ALU.subtract).then_inc(pair_ready, 1)
                nc.vector.scalar_tensor_tensor(out=spread[:], in0=stats[:, :, 2], scalar=EPS * D,
                                               in1=stats[:, :, 5], op0=ALU.add,
                                               op1=ALU.add).then_inc(pair_ready, 1)
                dve.wait_ge(pair_ready, 3 * (b + 1))
                nc.vector.tensor_scalar(mean[:], mean[:], 0.5, None, ALU.mult).then_inc(mean_ready, 1)
                nc.vector.scalar_tensor_tensor(out=diff[:], in0=diff[:], scalar=0.25, in1=diff[:],
                                               op0=ALU.mult, op1=ALU.mult).then_inc(mean_ready, 1)
                dve.wait_ge(mean_ready, 2 * (b + 1))
                nc.vector.scalar_tensor_tensor(out=var_eps[:], in0=spread[:], scalar=1.0 / D,
                                               in1=diff[:], op0=ALU.mult,
                                               op1=ALU.add).then_inc(eps_ready, 1)
                dve.wait_ge(rstd_ready, b + 1)
                nc.vector.scalar_tensor_tensor(out=shift[:], in0=mean[:], scalar=-1.0, in1=rstd[:],
                                               op0=ALU.mult, op1=ALU.mult).then_inc(shift_ready, 1)
                for j in range(PAIR):
                    last = nc.vector.tensor_scalar(norm[0][:, j, :], rows[1][:, j, :],
                                                   mean[:, j:j + 1], rstd[:, j:j + 1],
                                                   ALU.subtract, ALU.mult)
                last.then_inc(norm_ready[0], 1)

            def split_block(layer, b, first=False):
                of_h = (b - 1 if layer == 0 else BLOCKS - 1) if first == (layer == 1) else None
                for c in range(CHUNKS):
                    if layer == 0 and first and c < RING:
                        y_low(BLOCKS - RING + c)
                    chunk_low(c, chunks_before(layer, b) + c)
                    if layer == 0 and first and c == RING:
                        weights_low(2)
                    if of_h is not None and c == EVAC_AT + 1:
                        feat_low(act_t[:], h_split(of_h))
                    if of_h is not None and c == ROWS_READY_AT:
                        z_low(of_h)
                    if layer == 1 and not first and c == EVAC_AT + 1:
                        residuals(b - 1)
                    if layer == 1 and not first and c == ROWS_READY_AT:
                        normalize(b - 1)
                    if layer == 1 and first and c == SELF_AT - 2:
                        weights_low(3)
                    if c == SELF_AT - 1:
                        feat_low(feat_raw[:], self_split(layer, b))
                if layer == 1 and not first:
                    dve.wait_ge(out_stored[0], 16 * b)

            dve.wait_ge(head_hi_ready, 1)
            low(chunk_lo[0][:, :, HEAD], raw[0][:, :, HEAD],
                chunk_hi[0][:, :, HEAD]).then_inc(head_lo_ready, 1)
            weights_low(0)
            dve.wait_ge(hi_ready, 1)
            low(chunk_lo[0][:, :, REST], raw[0][:, :, REST],
                chunk_hi[0][:, :, REST]).then_inc(lo_ready, 1)
            for b in range(1, BLOCKS):
                if b >= RING:
                    y_low(b - RING)
                chunk_low(b, b)
                if b == RING:
                    weights_low(1)
            split_block(0, 0, first=True)
            with dve.Fori(1, BLOCKS) as b:
                split_block(0, b)
            split_block(1, 0, first=True)
            with dve.Fori(1, BLOCKS) as b:
                split_block(1, b)
            residuals(BLOCKS - 1)
            normalize(BLOCKS - 1)

        @block.gpsimd
        def _(pool):
            nc.gpsimd.memset(minus_half[:], -0.5).then_inc(minus_half_ready, 1)
            pool.wait_ge(minus_half_ready, 1)
            with pool.Fori(0, BLOCKS) as b:
                pool.wait_ge(eps_ready, b + 1)
                nc.gpsimd.tensor_tensor(out=rstd[:], in0=var_eps[:], in1=minus_half[:],
                                        op=ALU.pow).then_inc(rstd_ready, 1)

        @block.tensor
        def _(pe):
            def product(dst, stationary, moving, start, stop):
                (sh, sl), (mh, ml) = stationary, moving
                nc.tensor.matmul(dst, sh, mh, start=start, stop=False)
                nc.tensor.matmul(dst, sh, ml, start=False, stop=False)
                return nc.tensor.matmul(dst, sl, mh, start=False, stop=stop)

            def row_products(dst, hi, lo, tiles=range(TILES)):
                for j in tiles:
                    n = slice(j * P, (j + 1) * P)
                    for f in range(HALVES):
                        last = product(dst[:, j, :], (hi[:, f, n], lo[:, f, n]),
                                       (w_hi[0][:, f, :], w_lo[0][:, f, :]),
                                       f == 0, f == HALVES - 1)
                return last

            def make_y(b):
                pe.wait_ge(lo_ready, b + 1)
                if b >= 2:
                    pe.wait_ge(y_lo_ready, b - 1)
                row_products(rows[b % 2], chunk_hi[b % RING], chunk_lo[b % RING])\
                    .then_inc(chunk_used, 1)

            def make_z(b):
                pe.wait_ge(feat_lo_ready, h_split(b) + 1)
                row_products(rows[0], feat_hi, feat_lo).then_inc(feat_used, 1)

            def self_term(layer, b):
                pe.wait_ge(feat_lo_ready, self_split(layer, b) + 1)
                for half in range(HALVES):
                    g = slice(half * P, (half + 1) * P)
                    for f in range(HALVES):
                        last = product(acc[:, half, :], (w_hi[1][:, f, g], w_lo[1][:, f, g]),
                                       (feat_hi[:, f, :], feat_lo[:, f, :]), False, False)
                last.then_inc(feat_used, 1)

            def aggregate(layer, b, c):
                v_hi, v_lo = ((y_hi, y_lo), (z_hi, z_lo))[layer]
                pe.wait_ge(lo_ready, chunks_before(layer, b) + c + 1)
                for half in range(HALVES):
                    if c == 0 and not (layer == 0 and isinstance(b, int)):
                        pe.wait_ge(act_ready, HALVES * (blocks_before(layer, b) - 1) + half + 1)
                    g = slice(half * P, (half + 1) * P)
                    for j in range(CK):
                        k = c * CK + j
                        last = product(acc[:, half, :], (v_hi[:, k, g], v_lo[:, k, g]),
                                       (chunk_hi[c % RING][:, j, :], chunk_lo[c % RING][:, j, :]),
                                       k == 0, k == KT - 1)
                    if c == CHUNKS - 1 and half == 0:
                        last.then_inc(half_done, 1)
                last.then_inc(chunk_used, 1)

            def turn(b):
                for half in range(HALVES):
                    pe.wait_ge(resid_ready, HALVES * b + half + 1)
                    for j in range(TILES):
                        last = nc.tensor.transpose(rows[1][:, j, half * P:(half + 1) * P],
                                                   act_t[:, half, j * P:(j + 1) * P], identity[:])
                        if half == HALVES - 1 and j % PAIR == PAIR - 1:
                            last.then_inc(turned, 1)

            def block_products(layer, b, first=False):
                of_h = (b - 1 if layer == 0 else BLOCKS - 1) if first == (layer == 1) else None
                for c in range(CHUNKS):
                    if first and layer == 0 and c % CPB == 0:
                        pe.wait_ge(y_lo_ready, c // CPB + 1)
                    if first and layer == 1 and c == 0:
                        pe.wait_ge(z_lo_ready, BLOCKS - 1)
                    if first and layer == 1 and c == CHUNKS - CPB:
                        pe.wait_ge(z_lo_ready, BLOCKS)
                    aggregate(layer, b, c)
                    if c == ROWS_AT and of_h is not None:
                        if layer == 0:
                            pe.wait_ge(w_lo_ready, 3)
                        make_z(of_h)
                    if c == ROWS_AT and layer == 1 and not first:
                        turn(b - 1)
                    if c == SELF_AT:
                        if first:
                            pe.wait_ge(w_lo_ready, 2 * (layer + 1))
                        self_term(layer, b)
                if layer == 0 and first:
                    pe.wait_ge(y_lo_ready, BLOCKS)
                if layer == 0 and not first:
                    pe.wait_ge(z_lo_ready, b)
                if layer == 1 and not first:
                    pe.wait_ge(norm_ready[0], b)
                    pe.wait_ge(norm_ready[1], b)

            pe.wait_ge(head_lo_ready, 1)
            pe.wait_ge(w_lo_ready, 1)
            row_products(rows[0], chunk_hi[0], chunk_lo[0], range(PAIR))
            pe.wait_ge(lo_ready, 1)
            row_products(rows[0], chunk_hi[0], chunk_lo[0], range(PAIR, TILES))\
                .then_inc(chunk_used, 1)
            for b in range(1, BLOCKS):
                make_y(b)
            block_products(0, 0, first=True)
            with pe.Fori(1, BLOCKS) as b:
                block_products(0, b)
            block_products(1, 0, first=True)
            pe.wait_ge(const_landed, 48)
            with pe.Fori(1, BLOCKS) as b:
                block_products(1, b)
            turn(BLOCKS - 1)


def kernel(x, adj, L0_gnn_W1, L0_gnn_b1, L0_gnn_W2, L0_gnn_b2):
    import numpy as np
    import concourse.bacc as bacc
    from concourse.bass_utils import run_bass_kernel_spmd

    n, d = x.shape
    blocks, kt, halves = n // BLOCK, n // P, d // P
    ready = np.ascontiguousarray

    def weights(w):
        return ready(np.asarray(w).reshape(2, halves, P, d).transpose(0, 2, 1, 3))

    arrays = {
        "adj_t": ready(np.asarray(adj).reshape(blocks, BLOCK, kt // CK, CK, P)
                       .transpose(0, 2, 4, 3, 1)),
        "x_t": ready(np.asarray(x).reshape(blocks, BLOCK, halves, P).transpose(0, 3, 2, 1)),
        "w1": weights(L0_gnn_W1),
        "w2": weights(L0_gnn_W2),
        "b1": ready(np.asarray(L0_gnn_b1).reshape(halves, P).T),
        "b2": ready(np.asarray(L0_gnn_b2).reshape(halves, P).T),
        "ident": np.eye(P, dtype=np.float32),
    }
    nc = bacc.Bacc("TRN2", target_bir_lowering=False, num_devices=1)
    ins = {name: nc.dram_tensor(name, a.shape, F32, kind="ExternalInput").ap()
           for name, a in arrays.items()}
    h_t = nc.dram_tensor("h_t", arrays["x_t"].shape, F32).ap()
    out = nc.dram_tensor("out", (blocks, 2, P, BLOCK // P // 2, d), F32, kind="ExternalOutput").ap()
    graph_resnorm_kernel(nc, h_t=h_t, out=out, **ins)
    got = run_bass_kernel_spmd(nc, [arrays], core_ids=[0]).results[0]["out"]
    return ready(got.transpose(0, 1, 3, 2, 4).reshape(n, d))
```
